# Optimizing a Trainium2 kernel written in Bass

```python
import numpy as np
import jax
import jax.numpy as jnp

def _softmax(x, axis=-1):
    return jax.nn.softmax(x, axis=axis)

def _gelu(x):
    return jax.nn.gelu(x, approximate=True)

def _silu(x):
    return jax.nn.silu(x)

def _sigmoid(x):
    return jax.nn.sigmoid(x)

def _layernorm(x, axis=-1, eps=1e-05):
    m = jnp.mean(x, axis=axis, keepdims=True)
    v = jnp.var(x, axis=axis, keepdims=True)
    return (x - m) / jnp.sqrt(v + eps)

def _scatter_add(tgt, idx, src, axis=0):
    return tgt.at[idx].add(src)

def _segment_sum(src, seg, n):
    return jax.ops.segment_sum(src, seg, n)
kernel_name = 'mk_rec_standalone_d1_rec_r8_ea7a4e'

def setup_inputs(seed: int=0):
    np.random.seed(seed)
    _w = jnp.asarray

    def _rec_inputs():
        import jax
        import jax.numpy as jnp
        _rk = jax.random.key(seed)
        r_input = -0.000520686 + 1.00062 * jax.random.normal(jax.random.fold_in(_rk, 1), (512, 64, 16), jnp.float32)
        return r_input
    r_input = _rec_inputs()

    def _L0_rec_setup():
        import jax, jax.numpy as jnp
        import numpy as np
        BATCH, FIELDS, EMBED = (256, 64, 16)
        LAYERS = [128, 128, 128]
        key = jax.random.key(seed)
        ks = jax.random.split(key, 7)
        inp = {'input': jax.random.normal(ks[0], (BATCH, FIELDS, EMBED), dtype=jnp.float32)}
        in_ch = [FIELDS * FIELDS, FIELDS * LAYERS[0], FIELDS * LAYERS[1]]
        for i, (cin, cout) in enumerate(zip(in_ch, LAYERS)):
            scale = 1.0 / np.sqrt(cin)
            inp[f'W{i}'] = jax.random.uniform(ks[1 + 2 * i], (cout, cin), jnp.float32, -scale, scale)
            inp[f'b{i}'] = jax.random.uniform(ks[2 + 2 * i], (cout,), jnp.float32, -scale, scale)
        return inp
    _L0_rec_all = _L0_rec_setup()
    _L0_rec_in = {k: v for k, v in _L0_rec_all.items() if k in ('W0', 'b0', 'W1', 'b1', 'W2', 'b2')}
    del _L0_rec_all
    return {'r_input': r_input, 'L0_rec_W0': _L0_rec_in['W0'], 'L0_rec_b0': _L0_rec_in['b0'], 'L0_rec_W1': _L0_rec_in['W1'], 'L0_rec_b1': _L0_rec_in['b1'], 'L0_rec_W2': _L0_rec_in['W2'], 'L0_rec_b2': _L0_rec_in['b2']}

def reference(r_input, L0_rec_W0, L0_rec_b0, L0_rec_W1, L0_rec_b1, L0_rec_W2, L0_rec_b2):
    import jax
    import jax.numpy as jnp

    def _L0_rec_ref(input, W0, b0, W1, b1, W2, b2):
        import jax, jax.numpy as jnp
        import numpy as np
        BATCH, FIELDS, EMBED = (256, 64, 16)
        LAYERS = [128, 128, 128]
        params = [(W0, b0), (W1, b1), (W2, b2)]
        x_vec = input
        outs = []
        for W, b in params:
            z = jnp.einsum('bhd,bfd->bhfd', x_vec, input)
            B, h, f, d = z.shape
            z = z.reshape(B, h * f, d)
            x_vec = jnp.einsum('oc,bcd->bod', W, z) + b[None, :, None]
            outs.append(x_vec.sum(axis=2))
        return jnp.concatenate(outs, axis=1)
    y = _L0_rec_ref(r_input, L0_rec_W0, L0_rec_b0, L0_rec_W1, L0_rec_b1, L0_rec_W2, L0_rec_b2)
    return y

_drawn_inputs = setup_inputs


def setup_inputs(seed=0):
    import zlib

    import numpy as np

    out = dict(_drawn_inputs(seed))
    spreads = {}
    factors = {}
    for name, (base, spread) in spreads.items():
        noise = np.random.default_rng([zlib.crc32(name.encode()), seed]).standard_normal(out[name].shape)
        drawn = base * np.exp(spread * noise) if base else spread * noise
        out[name] = jnp.asarray(drawn.astype(out[name].dtype))
    for name, factor in factors.items():
        out[name] = (out[name] * factor).astype(out[name].dtype)
    return out
```

```python
from contextlib import ExitStack

import concourse.bass as bass
from concourse import mybir

F32 = mybir.dt.float32
F32R = mybir.dt.float32r
ALU = mybir.AluOpType
ACT = mybir.ActivationFunctionType
AX = mybir.AxisListType

B, F, D = 512, 64, 16
O = 128
P = 128
L = 3

TILE_B = P // D
TILES = 4
GROUP = TILES * P
GROUP_B = TILES * TILE_B
GROUPS = B // GROUP_B
QUARTERS = 4
QG = GROUPS // QUARTERS
QB = B // QUARTERS

ZT = F // 4 + 1
ZLAST = F // 2
ZSLOTS = 11

CF = 4
CHUNK = CF * O
CHUNKS = F // CF
YB = 4
HELPED = (1, 4, 6, 9, 12, 14)
HN = len(HELPED)
SUMMED = tuple(c for c in range(CHUNKS) if c not in HELPED)
SN = CF * len(SUMMED)
POOL_STEPS = HN + 1
HSLOTS = 3
LAYER2_AT = 11


def zslot(t):
    return t % ZSLOTS


def zuses(slot):
    return len(range(slot, ZT, ZSLOTS))


def cin_kernel(nc, x, w0, b0, w1, b1, w2, b2, out):
    with ExitStack() as ctx:
        def sb(name, shape, dt=F32):
            return ctx.enter_context(nc.sbuf_tensor(name, shape, dt))

        def ps(name, shape):
            return ctx.enter_context(nc.psum_tensor(name, shape, F32))

        def sem(name):
            return ctx.enter_context(nc.semaphore(name))

        w1h = sb("w1h", [P, CHUNKS, CHUNK], F32R)
        w1l = sb("w1l", [P, CHUNKS, CHUNK], F32R)
        w2t = sb("w2t", [P, F, O])
        gram = sb("gram", [P, F, QB])
        w0s = sb("w0s", [P, ZT, O])
        z = sb("z", [P, ZSLOTS, GROUP])
        xg = sb("xg", [P, GROUP])
        x1h = sb("x1h", [P, GROUP], F32R)
        x1l = sb("x1l", [P, GROUP], F32R)
        x0t = sb("x0t", [P, TILES, F])
        bd = sb("bd", [P, TILES, F, TILE_B])
        acc = sb("acc", [P, 2, CF, O])
        prod = sb("prod", [P, HSLOTS, CF, O])
        pacc = sb("pacc", [P, CF, O])
        fold = sb("fold", [P, 2, O])
        x2 = sb("x2", [P, 2, O])
        ident = sb("ident", [P, P])
        own = sb("own", [P, TILE_B])
        b0c = sb("b0c", [P, 1])
        b2c = sb("b2c", [P, 1])
        b0d = sb("b0d", [P, 1])
        b2d = sb("b2d", [P, 1])
        b1r = sb("b1r", [P, O])
        sums0 = sb("sums0", [P, (GROUPS + 1) * GROUP_B])
        sums1 = sb("sums1", [P, B])
        sums2 = sb("sums2", [P, B])

        w1raw = w2t[:].rearrange("p f o -> p (f o)")
        w2raw = gram[:].rearrange("p f b -> p (f b)")
        w0raw = w2raw[:, 0:F * F]
        w0pair = w2raw[:, F * F:F * F + ZT * P]
        outs = bd[:].rearrange("p t f b -> p (t f b)")[:, 0:(B // P) * L * O].rearrange(
            "p (r n) -> p r n", r=B // P)

        y = [ps(f"y{i}", [P, CHUNK]) for i in range(YB)]
        l0 = ps("l0", [P, GROUP])
        gp = ps("gp", [P, F, TILE_B])
        xt = ps("xt", [P, TILES, F])
        s1 = ps("s1", [P, TILE_B])
        l2 = xt[:].rearrange("p t f -> p (t f)")[:, 0:QB]

        w0_loaded = sem("w0_loaded")
        w1_loaded = sem("w1_loaded")
        w2_loaded = sem("w2_loaded")
        bias_loaded = sem("bias_loaded")
        ones_set = sem("ones_set")
        consts_made = sem("consts_made")
        pair_made = sem("pair_made")
        bias_made = sem("bias_made")
        prep_made = sem("prep_made")
        w1h_made = sem("w1h_made")
        xg_loaded = sem("xg_loaded")
        b_loaded = [sem(f"b_loaded{i}") for i in range(ZSLOTS)]
        z_made = sem("z_made")
        z_used = sem("z_used")
        xt_made = sem("xt_made")
        x0t_made = sem("x0t_made")
        bd_made = sem("bd_made")
        x1h_made = sem("x1h_made")
        x1l_made = sem("x1l_made")
        l0_used = sem("l0_used")
        y_made = sem("y_made")
        y_used = [sem(f"y_used{i}") for i in range(YB)]
        acc_step = sem("acc_step")
        prod_made = sem("prod_made")
        pool_step = sem("pool_step")
        x2_made = sem("x2_made")
        gp_made = sem("gp_made")
        gp_used = sem("gp_used")
        l2_made = sem("l2_made")
        l2_used = sem("l2_used")
        sums_made = sem("sums_made")
        turned = sem("turned")
        outs_made = [sem("outs_made0"), sem("outs_made1")]
        stored = sem("stored")

        W0_STEPS = -(-ZT // 4)
        PREP = [("w0", r, r % YB) for r in range(W0_STEPS)]
        PREP += [("w1", c, c % YB) for c in range(CHUNKS)]
        PREP += [("w2", c, c % YB) for c in range(CHUNKS)]

        def uses(steps, bank):
            return sum(b == bank for _, _, b in steps)

        def z_rows(t):
            return P if t < ZT - 1 else ZLAST

        def tile_added(tile):
            return SN * tile + 2 * SN

        def x2_ready(tile):
            return tile + 3

        def layer2_ready(tile):
            return tile + 3

        def pool_at(tile, step):
            return POOL_STEPS * tile + (POOL_STEPS + 1 + step)

        block = ctx.enter_context(nc.Block())

        @block.sync
        def _(sp):
            def front(n, first):
                if first:
                    rows = x[0:GROUP_B]
                else:
                    rows = x[bass.ds((n % GROUPS) * GROUP_B, GROUP_B), :, :]
                    sp.wait_ge(z_made, ZT * n)
                    sp.wait_ge(xt_made, n)
                for half in range(2):
                    sp.dma_start(xg[half * F:(half + 1) * F, :].rearrange("f (b d) -> f b d", d=D),
                                 rows.rearrange("b f d -> f b d")).then_inc(xg_loaded, 16)
                sp.wait_ge(xg_loaded, 32 * n + 32)
                for t in range(ZT):
                    if t >= ZSLOTS:
                        sp.wait_ge(z_used, ZT * n + (t - ZSLOTS + 1))
                    elif t == 0 and not first:
                        sp.wait_ge(z_used, ZT * n)
                    shift, slot = 2 * t, zslot(t)
                    if t < ZT - 1:
                        for half in range(2):
                            sp.dma_start(z[half * F:(half + 1) * F, slot, :],
                                         xg[shift + half:shift + half + F, :]).then_inc(b_loaded[slot], 16)
                    else:
                        sp.dma_start(z[0:ZLAST, slot, :], xg[shift:shift + ZLAST, :]).then_inc(b_loaded[slot], 32)

            front(0, True)
            with sp.Fori(0, QUARTERS) as q:
                with sp.Fori(0, QG) as i:
                    front(q * QG + i + 1, False)
            for r in range(B // P):
                sp.wait_ge(outs_made[r % 2], r // 2 + 1)
                sp.dma_start(out[r * P:(r + 1) * P, :], outs[:, r, :]).then_inc(stored, 16)
            sp.wait_ge(stored, 16 * (B // P))

        @block.gpsimd
        def _(pool):
            pool.sem_inc(pool_step, POOL_STEPS + 1)
            pool.sem_inc(x2_made, 2)
            nc.gpsimd.memset(ident[:], 0.0)
            nc.gpsimd.memset(own[:], 1.0).then_inc(ones_set, 1)
            pool.wait_ge(ones_set, 1)
            nc.gpsimd.affine_select(out=ident[:], in_=ident[:], compare_op=ALU.not_equal, fill=1.0, base=0,
                                    pattern=[[-1, P]], channel_multiplier=1).then_inc(ones_set, 1)
            nc.gpsimd.affine_select(out=own[:], in_=own[:], compare_op=ALU.is_ge, fill=0.0, base=0,
                                    pattern=[[-D, TILE_B]], channel_multiplier=1).then_inc(ones_set, 1)
            pool.wait_ge(ones_set, 3)
            nc.gpsimd.affine_select(out=own[:], in_=own[:], compare_op=ALU.is_ge, fill=0.0, base=D - 1,
                                    pattern=[[D, TILE_B]], channel_multiplier=-1).then_inc(consts_made, 1)

            def product(n, t):
                slot, rows = zslot(t), z_rows(t)
                of_group = len(range(slot, ZT, ZSLOTS))
                pool.wait_ge(b_loaded[slot], 32 * (of_group * n + t // ZSLOTS + 1))
                nc.gpsimd.tensor_tensor(z[0:rows, slot, :], z[0:rows, slot, :], xg[0:rows, :],
                                        ALU.mult).then_inc(z_made, 1)

            def add_products(tile, h):
                pool.wait_ge(prod_made, HN * tile + (HN + h + 1))
                pool.wait_ge(pool_step, pool_at(tile, h - 1))
                if h == 1:
                    nc.gpsimd.tensor_tensor(pacc[:], prod[:, 0], prod[:, 1], ALU.add).then_inc(pool_step, 1)
                else:
                    nc.gpsimd.tensor_tensor(pacc[:], pacc[:], prod[:, h % HSLOTS], ALU.add).then_inc(pool_step, 1)

            def combine(tile, j):
                pool.wait_ge(acc_step, tile_added(tile))
                pool.wait_ge(pool_step, pool_at(tile, HN - 1))
                nc.gpsimd.tensor_tensor(pacc[:], pacc[:], acc[:, j % 2], ALU.add).then_inc(pool_step, 1)
                pool.wait_ge(pool_step, pool_at(tile, HN))
                nc.gpsimd.tensor_tensor(fold[:], pacc[:, 0:2], pacc[:, 2:4], ALU.add).then_inc(pool_step, 1)
                pool.wait_ge(pool_step, pool_at(tile, HN + 1))
                pool.wait_ge(gp_made, layer2_ready(tile - 2))
                nc.gpsimd.tensor_tensor(x2[:, j % 2], fold[:, 0], fold[:, 1], ALU.add).then_inc(x2_made, 1)

            for t in range(ZT):
                product(0, t)
            with pool.Fori(0, QUARTERS) as q:
                with pool.Fori(0, QG) as i:
                    n = q * QG + i
                    ahead = list(range(ZT))
                    for j in range(TILES):
                        tile = n * TILES + j
                        for h in range(1, HN):
                            add_products(tile, h)
                            if h in (2, 3, 4) and len(ahead) > ZT - ZSLOTS:
                                product(n + 1, ahead.pop(0))
                        combine(tile, j)
                    for t in ahead:
                        product(n + 1, t)

        @block.scalar
        def _(act):
            act.sem_inc(gp_used, 1)
            act.sem_inc(prod_made, HN)
            act.dma_start(w0raw, w0).then_inc(w0_loaded, 16)
            act.dma_start(b0c[:], b0.rearrange("(p a) -> p a", a=1)).then_inc(bias_loaded, 16)
            act.dma_start(b2c[:], b2.rearrange("(p a) -> p a", a=1)).then_inc(bias_loaded, 16)
            act.dma_start(b1r[:], b1.rearrange("(a o) -> a o", a=1).to_broadcast((P, O))).then_inc(bias_loaded, 16)
            act.dma_start(w1raw, w1).then_inc(w1_loaded, 16)

            def front(n):
                act.wait_ge(xt_made, n + 1)
                act.wait_ge(acc_step, tile_added(n * TILES - 1))
                act.wait_ge(prod_made, HN * TILES * n + HN)
                nc.scalar.copy(x0t[:], xt[:]).then_inc(x0t_made, 1)
                act.wait_ge(z_used, ZT * n + ZT)
                nc.scalar.activation(x1h[:], l0[:], ACT.Identity, bias=b0c[:, 0:1]).then_inc(x1h_made, 1)

            def layer2_out(tile, i, j):
                act.wait_ge(gp_made, layer2_ready(tile))
                nc.scalar.copy(gram[:, :, bass.ds(i * GROUP_B + j * TILE_B, TILE_B)], gp[:])
                nc.scalar.copy(sums1[:, bass.ds(tile * TILE_B, TILE_B)], s1[:]).then_inc(gp_used, 1)

            def multiply(tile, j, c):
                h = HELPED.index(c)
                act.wait_ge(y_made, CHUNKS * tile + c + 1)
                before = (h - HSLOTS) % HN
                act.wait_ge(pool_step, pool_at(tile, max(before, 1) - (POOL_STEPS if h < HSLOTS else 0)))
                for k in range(CF):
                    f = CF * c + k
                    last = nc.scalar.activation(prod[:, h % HSLOTS, k, :], y[c % YB][:, k * O:(k + 1) * O],
                                                ACT.Copy, scale=x0t[:, j, f:f + 1])
                last.then_inc(prod_made, 1)

            act.wait_ge(bias_loaded, 48)
            for k, (what, r, bank) in enumerate(PREP):
                if what == "w1" and r == 0:
                    act.dma_start(w2raw, w2).then_inc(w2_loaded, 16)
                    front(0)
                act.wait_ge(prep_made, k + 1)
                if what == "w0" and r < W0_STEPS - 1:
                    nc.scalar.copy(w0s[:, 4 * r:4 * r + 4, :], y[bank][:].rearrange("p (t o) -> p t o", o=O)) \
                        .then_inc(y_used[bank], 1)
                elif what == "w0":
                    nc.scalar.copy(w0s[0:ZLAST, ZT - 1, :], y[bank][0:ZLAST, 0:O]).then_inc(y_used[bank], 1)
                elif what == "w1":
                    nc.scalar.copy(w1h[:, r, :], y[bank][:]).then_inc(w1h_made, 1)
                else:
                    nc.scalar.copy(w2t[:, CF * r:CF * r + CF, :], y[bank][:].rearrange("p (f o) -> p f o", o=O)) \
                        .then_inc(y_used[bank], 1)

            act.wait_ge(bias_made, 1)
            with act.Fori(0, QUARTERS) as q:
                with act.Fori(0, QG) as i:
                    n = q * QG + i
                    act.wait_ge(x0t_made, n + 1)
                    for j in range(TILES):
                        tile = n * TILES + j
                        for c in range(CHUNKS):
                            if c in HELPED:
                                multiply(tile, j, c)
                            if c == LAYER2_AT and j > 0:
                                layer2_out(tile - 1, i, j - 1)
                    front(n + 1)
                    layer2_out(n * TILES + TILES - 1, i, TILES - 1)
                act.wait_ge(l2_made, q + 1)
                nc.scalar.activation(sums2[:, bass.ds(q * QB, QB)], l2, ACT.Identity,
                                     bias=b2d[:, 0:1]).then_inc(l2_used, 1)
            for r in range(0, B // P, 2):
                act.wait_ge(turned, r + 1)
                nc.scalar.copy(outs[:, r, :], y[r][:, 0:L * O]).then_inc(outs_made[0], 1)

        @block.vector
        def _(dve):
            dve.sem_inc(acc_step, SN)

            dve.wait_ge(w0_loaded, 16)
            for s in range(F // 2 + 1):
                to = s * F
                if s == 0:
                    nc.vector.tensor_copy(w0pair[:, 0:F], w0raw[:, 0:F * F:F + 1])
                    continue
                whole = F - s if s < F // 2 else ZLAST
                a = w0raw[:, s:s + (whole - 1) * (F + 1) + 1:F + 1]
                b = w0raw[:, s * F:s * F + (whole - 1) * (F + 1) + 1:F + 1]
                last = nc.vector.tensor_tensor(w0pair[:, to:to + whole], a, b, ALU.add)
                if s < F // 2:
                    r = F - s
                    a = w0raw[:, r * F:r * F + (s - 1) * (F + 1) + 1:F + 1]
                    b = w0raw[:, r:r + (s - 1) * (F + 1) + 1:F + 1]
                    last = nc.vector.tensor_tensor(w0pair[:, to + r:to + F], a, b, ALU.add)
            last.then_inc(pair_made, 1)
            dve.wait_ge(bias_loaded, 48)
            nc.vector.tensor_scalar(b0d[:], b0c[:], float(D), None, ALU.mult)
            nc.vector.tensor_scalar(b2d[:], b2c[:], float(D), None, ALU.mult).then_inc(bias_made, 1)

            def own_rows(n, j, first):
                if not first:
                    dve.wait_ge(gp_made, layer2_ready(n * TILES + (j - TILES)))
                shape = [P, F, TILE_B]
                nc.vector.tensor_tensor(bd[:, j], x0t[:, j, :].unsqueeze(2).to_broadcast(shape),
                                        own[:].unsqueeze(1).to_broadcast(shape), ALU.mult).then_inc(bd_made, 1)

            def front(n, first):
                dve.wait_ge(x0t_made, n + 1)
                for j in range(TILES - 1):
                    own_rows(n, j, first)
                dve.wait_ge(x1h_made, n + 1)
                nc.vector.scalar_tensor_tensor(out=x1l[:], in0=l0[:], scalar=b0c[:, 0:1], in1=x1h[:].bitcast(F32),
                                               op0=ALU.add, op1=ALU.subtract).then_inc(x1l_made, 1)
                to = sums0[:, 0:GROUP_B] if first else sums0[:, bass.ds(n * GROUP_B, GROUP_B)]
                nc.vector.tensor_reduce(to, l0[:].rearrange("p (b d) -> p b d", d=D), AX.X,
                                        ALU.add).then_inc(l0_used, 1)
                own_rows(n, TILES - 1, first)

            def add_fields(tile, j, c):
                m = SUMMED.index(c)
                if m == 0:
                    dve.wait_ge(x2_made, x2_ready(tile - 2))
                dve.wait_ge(y_made, CHUNKS * tile + c + 1)
                for k in range(CF):
                    f = CF * c + k
                    to, of = acc[:, j % 2, k, :], y[c % YB][:, k * O:(k + 1) * O]
                    if m > 0 and k % 2 == 0:
                        dve.wait_ge(acc_step, SN * tile + (SN + CF * (m - 1) + k + 2))
                    if m == 0 and k > 0:
                        ins = nc.vector.tensor_scalar(to, of, x0t[:, j, f:f + 1], None, ALU.mult)
                    else:
                        ins = nc.vector.scalar_tensor_tensor(out=to, in0=of, scalar=x0t[:, j, f:f + 1],
                                                             in1=b1r[:] if m == 0 else to,
                                                             op0=ALU.mult, op1=ALU.add)
                    ins.then_inc(acc_step, 1)

            dve.wait_ge(consts_made, 1)
            front(0, True)
            for k, (what, r, bank) in enumerate(PREP):
                if what == "w1":
                    dve.wait_ge(w1h_made, r + 1)
                    nc.vector.tensor_tensor(w1l[:, r, :], y[bank][:], w1h[:, r, :].bitcast(F32),
                                            ALU.subtract).then_inc(y_used[bank], 1)
            with dve.Fori(0, QUARTERS) as q:
                with dve.Fori(0, QG) as i:
                    n = q * QG + i
                    for j in range(TILES):
                        for c in SUMMED:
                            add_fields(n * TILES + j, j, c)
                    front(n + 1, False)
            dve.wait_ge(l0_used, GROUPS + 1)
            nc.vector.tensor_scalar(sums0[:, 0:B], sums0[:, 0:B], b0d[:, 0:1], None, ALU.add).then_inc(sums_made, 1)
            for r in range(1, B // P, 2):
                dve.wait_ge(turned, r + 1)
                nc.vector.tensor_copy(outs[:, r, :], y[r][:, 0:L * O]).then_inc(outs_made[1], 1)

        @block.tensor
        def _(pe):
            pe.sem_inc(gp_made, 2)

            def front(n, first):
                if not first:
                    pe.wait_ge(l0_used, n)
                for t in range(ZT):
                    rows = z_rows(t)
                    pe.wait_ge(z_made, ZT * n + t + 1)
                    nc.tensor.matmul(l0[:], w0s[0:rows, t, :], z[0:rows, zslot(t), :], start=(t == 0),
                                     stop=(t == ZT - 1)).then_inc(z_used, 1)
                    if t == 2:
                        for j in range(TILES):
                            last = nc.tensor.transpose(xt[:, j, :], xg[0:F, j * P:(j + 1) * P], ident[0:F, 0:F])
                        last.then_inc(xt_made, 1)

            def layer2(tile, j):
                pe.wait_ge(x2_made, x2_ready(tile))
                pe.wait_ge(bd_made, tile + 1)
                pe.wait_ge(gp_used, tile + 1)
                nc.tensor.matmul(gp[:].rearrange("p f b -> p (f b)"), x2[:, j % 2],
                                 bd[:, j].rearrange("p f b -> p (f b)"), start=True, stop=True)
                nc.tensor.matmul(s1[:], x2[:, j % 2], own[:], start=True, stop=True).then_inc(gp_made, 1)

            def chunk(tile, j, c):
                before, late = (c - YB) % CHUNKS, c < YB
                if before in HELPED:
                    value = HN * tile + (HN + HELPED.index(before) + 1) - (HN if late else 0)
                    pe.wait_ge(prod_made, value)
                else:
                    value = SN * tile + (SN + CF * SUMMED.index(before) + CF) - (SN if late else 0)
                    pe.wait_ge(acc_step, value)
                cols = slice(j * P, (j + 1) * P)
                nc.tensor.matmul(y[c % YB][:], x1h[:, cols], w1h[:, c, :], start=True, stop=False)
                nc.tensor.matmul(y[c % YB][:], x1h[:, cols], w1l[:, c, :], start=False, stop=False)
                nc.tensor.matmul(y[c % YB][:], x1l[:, cols], w1h[:, c, :], start=False, stop=True) \
                    .then_inc(y_made, 1)

            pe.wait_ge(consts_made, 1)
            for k, (what, r, bank) in enumerate(PREP):
                if (what, r) == ("w0", 0):
                    pe.wait_ge(pair_made, 1)
                if (what, r) == ("w1", 0):
                    for i in range(YB):
                        pe.wait_ge(y_used[i], uses(PREP[:k], i))
                    front(0, True)
                    pe.wait_ge(w1_loaded, 16)
                if (what, r) == ("w2", 0):
                    pe.wait_ge(w2_loaded, 16)
                if uses(PREP[:k], bank):
                    pe.wait_ge(y_used[bank], uses(PREP[:k], bank))
                if what == "w0":
                    for t in range(4 * r, min(4 * r + 4, ZT)):
                        rows = z_rows(t)
                        last = nc.tensor.transpose(y[bank][0:rows, (t % 4) * O:(t % 4 + 1) * O],
                                                   w0pair[:, t * P:t * P + rows], ident[:])
                else:
                    raw = (w1raw if what == "w1" else w2raw).rearrange("o (h f) -> o f h", f=F)
                    for k4 in range(CF):
                        last = nc.tensor.transpose(y[bank][:, k4 * O:(k4 + 1) * O], raw[:, CF * r + k4, :], ident[:])
                last.then_inc(prep_made, 1)
            for i in range(YB):
                pe.wait_ge(y_used[i], uses(PREP, i))

            with pe.Fori(0, QUARTERS) as q:
                with pe.Fori(0, QG) as i:
                    n = q * QG + i
                    pe.wait_ge(x1h_made, n + 1)
                    pe.wait_ge(x1l_made, n + 1)
                    for j in range(TILES):
                        for c in range(CHUNKS):
                            chunk(n * TILES + j, j, c)
                            if c == LAYER2_AT and j > 0:
                                layer2(n * TILES + j - 1, j - 1)
                    front(n + 1, False)
                    layer2(n * TILES + TILES - 1, TILES - 1)
                pe.wait_ge(gp_used, q * (QG * TILES) + QG * TILES + 1)
                pe.wait_ge(x0t_made, q * QG + QG + 1)
                for f in range(F):
                    last = nc.tensor.matmul(l2, w2t[:, f, :], gram[:, f, :], start=(f == 0), stop=(f == F - 1))
                last.then_inc(l2_made, 1)

            pe.wait_ge(sums_made, 1)
            pe.wait_ge(l2_used, QUARTERS)
            for r in range(B // P):
                for k, sums in enumerate((sums0, sums1, sums2)):
                    last = nc.tensor.transpose(y[r][:, k * O:(k + 1) * O], sums[:, r * P:(r + 1) * P], ident[:])
                last.then_inc(turned, 1)


_INS = ["r_input", "L0_rec_W0", "L0_rec_b0", "L0_rec_W1", "L0_rec_b1", "L0_rec_W2", "L0_rec_b2"]
_OUTS = [((B, L * O), "float32")]


def kernel(**inputs):
    import numpy as _np
    import concourse.bacc as _bacc
    from concourse import mybir as _mybir
    from concourse.bass_utils import run_bass_kernel_spmd as _run

    nc = _bacc.Bacc("TRN2", target_bir_lowering=False, num_devices=1)
    arrays, args = {}, []
    for name in _INS:
        a = _np.ascontiguousarray(inputs[name])
        arrays[f"in_{name}_dram"] = a
        args.append(nc.dram_tensor(f"in_{name}_dram", a.shape, _mybir.dt.from_np(a.dtype), kind="ExternalInput").ap())
    for i, (shape, dtype) in enumerate(_OUTS):
        dt = _mybir.dt.from_np(_np.dtype(dtype))
        args.append(nc.dram_tensor(f"out_{i}_dram", shape, dt, kind="ExternalOutput").ap())
    cin_kernel(nc, *args)
    r = _run(nc, [arrays], core_ids=[0])
    got = tuple(r.results[0][f"out_{i}_dram"] for i in range(len(_OUTS)))
    return got[0]
```

```python
from contextlib import ExitStack

import concourse.bass as bass
from concourse import mybir

F32 = mybir.dt.float32
F32R = mybir.dt.float32r
ALU = mybir.AluOpType
ACT = mybir.ActivationFunctionType
AX = mybir.AxisListType

B, F, D = 512, 64, 16
O = 128
P = 128
L = 3

TILE_B = P // D
TILES = 4
GROUP = TILES * P
GROUP_B = TILES * TILE_B
GROUPS = B // GROUP_B
QUARTERS = 4
QG = GROUPS // QUARTERS
QB = B // QUARTERS

ZT = F // 4 + 1
ZLAST = F // 2
ZSLOTS = 6
ZPARTS = 4

CF = 4
CHUNK = CF * O
CHUNKS = F // CF
YB = 4
HELPED = (1, 4, 6, 9, 12, 14)
HN = len(HELPED)
SUMMED = tuple(c for c in range(CHUNKS) if c not in HELPED)
SN = CF * len(SUMMED)
HSLOTS = 3
POOL_STEPS = HN + 1

LAYER2_AT = 10
QUARTER_PARTS = 8
QUARTER_AT = [CHUNKS + 2 + k for k in range(QUARTER_PARTS)]
AHEAD_AT = [10 + t * 46 // (ZT - 1) for t in range(ZT)]
PARTS_BEFORE = 4
TURN_AT = 30
SPLIT_AT = AHEAD_AT[-1] + 1
W2_AT = 8
PRODUCTS_IN = (6, 5, 5, 1)


def zslot(t):
    return t % ZSLOTS


def last_in(t, slots):
    return max(range(t % slots, ZT, slots))


def cin_kernel(nc, x, w0, b0, w1, b1, w2, b2, out):
    with ExitStack() as ctx:
        def sb(name, shape, dt=F32):
            return ctx.enter_context(nc.sbuf_tensor(name, shape, dt))

        def ps(name, shape):
            return ctx.enter_context(nc.psum_tensor(name, shape, F32))

        def sem(name):
            return ctx.enter_context(nc.semaphore(name))

        w1h = sb("w1h", [P, CHUNKS, CHUNK], F32R)
        w1l = sb("w1l", [P, CHUNKS, CHUNK], F32R)
        w2t = sb("w2t", [P, F, O])
        gram = sb("gram", [P, F, QB])
        w0h = sb("w0h", [P, ZT, O], F32R)
        w0l = sb("w0l", [P, ZT, O], F32R)
        z = sb("z", [P, ZSLOTS, GROUP])
        zh = sb("zh", [P, ZPARTS, GROUP], F32R)
        zl = sb("zl", [P, ZPARTS, GROUP], F32R)
        xg = sb("xg", [P, GROUP])
        x1h = sb("x1h", [P, GROUP], F32R)
        x1l = sb("x1l", [P, GROUP], F32R)
        x0t = sb("x0t", [P, TILES, F])
        bd = sb("bd", [P, 2, F, TILE_B])
        acc = sb("acc", [P, 2, CF, O])
        prod = sb("prod", [P, HSLOTS, CF, O])
        pacc = sb("pacc", [P, CF, O])
        fold = sb("fold", [P, 2, O])
        x2 = sb("x2", [P, 2, O])
        ident = sb("ident", [P, P])
        own = sb("own", [P, TILE_B])
        b0c = sb("b0c", [P, 1])
        b2c = sb("b2c", [P, 1])
        b0d = sb("b0d", [P, 1])
        b2d = sb("b2d", [P, 1])
        b1r = sb("b1r", [P, O])
        sums0 = sb("sums0", [P, B])
        sums1 = sb("sums1", [P, B])
        sums2 = sb("sums2", [P, QB + B])

        w1raw = w2t[:].rearrange("p f o -> p (f o)")
        w2raw = gram[:].rearrange("p f b -> p (f b)")
        w0raw = w2raw[:, 0:F * F]
        w0pair = w2raw[:, F * F:F * F + ZT * P]
        outs = z[:].rearrange("p t n -> p (t n)")[:, 0:(B // P) * L * O].rearrange(
            "p (r n) -> p r n", r=B // P)

        y = [ps(f"y{i}", [P, CHUNK]) for i in range(YB)]
        l0 = ps("l0", [P, GROUP])
        gp = ps("gp", [P, F * TILE_B])
        xt = ps("xt", [P, TILES, F])
        s1 = ps("s1", [P, CHUNK])
        l2 = xt[:].rearrange("p t f -> p (t f)")[:, 0:QB]

        w0_loaded = sem("w0_loaded")
        w1_loaded = sem("w1_loaded")
        w2_loaded = sem("w2_loaded")
        bias_loaded = sem("bias_loaded")
        ones_set = sem("ones_set")
        consts_made = sem("consts_made")
        pair_made = sem("pair_made")
        bias_made = sem("bias_made")
        prep_made = sem("prep_made")
        wh_made = sem("wh_made")
        w2_turned = sem("w2_turned")
        w2_kept = sem("w2_kept")
        xg_loaded = sem("xg_loaded")
        b_loaded = [sem(f"b_loaded{i}") for i in range(ZSLOTS)]
        z_made = sem("z_made")
        zh_made = sem("zh_made")
        zl_made = sem("zl_made")
        z_used = sem("z_used")
        xt_made = sem("xt_made")
        x0t_made = sem("x0t_made")
        bd_made = sem("bd_made")
        x1h_made = sem("x1h_made")
        x1l_made = sem("x1l_made")
        l0_used = sem("l0_used")
        y_made = sem("y_made")
        y_used = [sem(f"y_used{i}") for i in range(YB)]
        acc_step = sem("acc_step")
        prod_made = sem("prod_made")
        pool_step = sem("pool_step")
        x2_made = sem("x2_made")
        gp_made = sem("gp_made")
        gp_used = sem("gp_used")
        l2_made = sem("l2_made")
        l2_used = sem("l2_used")
        sums_made = sem("sums_made")
        turned = sem("turned")
        outs_made = [sem("outs_made0"), sem("outs_made1")]
        stored = sem("stored")

        W0_STEPS = -(-ZT // 4)
        PREP = [("w0", r, r % YB) for r in range(W0_STEPS)]
        PREP += [("w1", c, c % YB) for c in range(CHUNKS)]

        def uses(steps, bank):
            return sum(b == bank for _, _, b in steps)

        def weights(of_w0, of_w1, what, r, bank):
            if what == "w1":
                return of_w1[:, r, :], y[bank][:]
            if r < W0_STEPS - 1:
                return of_w0[:, 4 * r:4 * r + 4, :], y[bank][:].rearrange("p (t o) -> p t o", o=O)
            return of_w0[0:ZLAST, ZT - 1, :], y[bank][0:ZLAST, 0:O]

        def z_rows(t):
            return P if t < ZT - 1 else ZLAST

        def tile_added(tile):
            return SN * tile + 2 * SN

        def x2_ready(tile):
            return tile + 3

        def layer2_ready(tile):
            return tile + 3

        def pool_at(tile, step):
            return POOL_STEPS * tile + (POOL_STEPS + 1 + step)

        FIRST, LAST = slice(0, TILES - 1), slice(TILES - 1, TILES)

        def columns(tiles):
            return slice(tiles.start * P, tiles.stop * P)

        def groups(engine, body):
            body(0, "first")
            with engine.Fori(1, GROUPS - 1) as n:
                body(n, "inner")
            body(GROUPS - 1, "last")

        block = ctx.enter_context(nc.Block())

        @block.sync
        def _(sp):
            def front(n, first):
                if first:
                    rows = x[0:GROUP_B]
                else:
                    rows = x[bass.ds(n * GROUP_B, GROUP_B), :, :]
                    sp.wait_ge(z_made, ZT * n)
                    sp.wait_ge(xt_made, n)
                for half in range(2):
                    sp.dma_start(xg[half * F:(half + 1) * F, :].rearrange("f (b d) -> f b d", d=D),
                                 rows.rearrange("b f d -> f b d")).then_inc(xg_loaded, 16)
                sp.wait_ge(xg_loaded, 32 * n + 32)
                for t in range(ZT):
                    if t >= ZSLOTS:
                        sp.wait_ge(zl_made, ZT * n + (t - ZSLOTS + 1))
                    elif not first:
                        sp.wait_ge(zl_made, ZT * (n - 1) + (last_in(t, ZSLOTS) + 1))
                    shift, slot = 2 * t, zslot(t)
                    if t < ZT - 1:
                        for half in range(2):
                            sp.dma_start(z[half * F:(half + 1) * F, slot, :],
                                         xg[shift + half:shift + half + F, :]).then_inc(b_loaded[slot], 16)
                    else:
                        sp.dma_start(z[0:ZLAST, slot, :], xg[shift:shift + ZLAST, :]).then_inc(b_loaded[slot], 32)

            front(0, True)
            with sp.Fori(1, GROUPS) as n:
                front(n, False)
            for r in range(B // P):
                sp.wait_ge(outs_made[r % 2], r // 2 + 1)
                sp.dma_start(out[r * P:(r + 1) * P, :], outs[:, r, :]).then_inc(stored, 16)
            sp.wait_ge(stored, 16 * (B // P))

        @block.gpsimd
        def _(pool):
            pool.sem_inc(pool_step, POOL_STEPS + 1)
            pool.sem_inc(x2_made, 2)
            nc.gpsimd.memset(ident[:], 0.0)
            nc.gpsimd.memset(own[:], 1.0).then_inc(ones_set, 1)
            pool.wait_ge(ones_set, 1)
            nc.gpsimd.affine_select(out=ident[:], in_=ident[:], compare_op=ALU.not_equal, fill=1.0, base=0,
                                    pattern=[[-1, P]], channel_multiplier=1).then_inc(ones_set, 1)
            nc.gpsimd.affine_select(out=own[:], in_=own[:], compare_op=ALU.is_ge, fill=0.0, base=0,
                                    pattern=[[-D, TILE_B]], channel_multiplier=1).then_inc(ones_set, 1)
            pool.wait_ge(ones_set, 3)
            nc.gpsimd.affine_select(out=own[:], in_=own[:], compare_op=ALU.is_ge, fill=0.0, base=D - 1,
                                    pattern=[[D, TILE_B]], channel_multiplier=-1).then_inc(consts_made, 1)

            def product(n, t):
                slot, rows = zslot(t), z_rows(t)
                of_group = len(range(slot, ZT, ZSLOTS))
                pool.wait_ge(b_loaded[slot], 32 * (of_group * n + t // ZSLOTS + 1))
                nc.gpsimd.tensor_tensor(z[0:rows, slot, :], z[0:rows, slot, :], xg[0:rows, :],
                                        ALU.mult).then_inc(z_made, 1)

            def add_products(tile, h):
                pool.wait_ge(prod_made, HN * tile + (HN + h + 1))
                pool.wait_ge(pool_step, pool_at(tile, h - 1))
                if h == 1:
                    nc.gpsimd.tensor_tensor(pacc[:], prod[:, 0], prod[:, 1], ALU.add).then_inc(pool_step, 1)
                else:
                    nc.gpsimd.tensor_tensor(pacc[:], pacc[:], prod[:, h % HSLOTS], ALU.add).then_inc(pool_step, 1)

            def combine(tile, slot):
                pool.wait_ge(acc_step, tile_added(tile))
                pool.wait_ge(pool_step, pool_at(tile, HN - 1))
                nc.gpsimd.tensor_tensor(pacc[:], pacc[:], acc[:, slot], ALU.add).then_inc(pool_step, 1)
                pool.wait_ge(pool_step, pool_at(tile, HN))
                nc.gpsimd.tensor_tensor(fold[:], pacc[:, 0:2], pacc[:, 2:4], ALU.add).then_inc(pool_step, 1)
                pool.wait_ge(pool_step, pool_at(tile, HN + 1))
                pool.wait_ge(gp_made, layer2_ready(tile - 2))
                nc.gpsimd.tensor_tensor(x2[:, slot], fold[:, 0], fold[:, 1], ALU.add).then_inc(x2_made, 1)

            def body(n, kind):
                ahead = iter(range(ZT))
                for j in range(TILES):
                    tile = n * TILES + j
                    mine = PRODUCTS_IN[j] if kind != "last" else 0
                    for _ in range(min(mine, 2)):
                        product(n + 1, next(ahead))
                    if kind != "first" or j > 0:
                        combine(tile - 1, (j - 1) % 2)
                    for h in range(1, HN):
                        if 2 + h <= mine:
                            product(n + 1, next(ahead))
                        add_products(tile, h)

            for t in range(ZT):
                product(0, t)
            groups(pool, body)
            combine(GROUPS * TILES - 1, 1)

        @block.scalar
        def _(act):
            act.sem_inc(gp_used, 1)
            act.sem_inc(l2_used, 1)
            act.sem_inc(prod_made, HN)

            def load(to, of, loaded):
                part = F * O // 8
                for k in range(8):
                    act.dma_start(to[:, k * part:(k + 1) * part], of[:, k * part:(k + 1) * part]).then_inc(loaded, 16)

            act.dma_start(w0raw, w0).then_inc(w0_loaded, 16)
            act.dma_start(b0c[:], b0.rearrange("(p a) -> p a", a=1)).then_inc(bias_loaded, 16)
            act.dma_start(b2c[:], b2.rearrange("(p a) -> p a", a=1)).then_inc(bias_loaded, 16)
            act.dma_start(b1r[:], b1.rearrange("(a o) -> a o", a=1).to_broadcast((P, O))).then_inc(bias_loaded, 16)
            load(w1raw, w1, w1_loaded)

            def upper_product(n, t):
                rows = z_rows(t)
                act.wait_ge(z_made, ZT * n + t + 1)
                if t >= ZPARTS:
                    act.wait_ge(z_used, ZT * n + (t - ZPARTS + 1))
                elif not isinstance(n, int) or n > 0:
                    act.wait_ge(z_used, ZT * (n - 1) + (last_in(t, ZPARTS) + 1))
                nc.scalar.copy(zh[0:rows, t % ZPARTS, :], z[0:rows, zslot(t), :]).then_inc(zh_made, 1)

            def fields(n, tiles, first):
                act.wait_ge(xt_made, n + 1)
                if not first:
                    act.wait_ge(acc_step, tile_added((n - 1) * TILES + (tiles.stop - 1)))
                    act.wait_ge(prod_made, HN * TILES * n - HN * TILES + HN * (tiles.stop + 1))
                nc.scalar.copy(x0t[:, tiles, :], xt[:, tiles, :]).then_inc(x0t_made, 1)

            def upper(n, tiles, first):
                if tiles == FIRST:
                    act.wait_ge(z_used, ZT * n + ZT)
                else:
                    act.wait_ge(x1l_made, 2 * n + 1)
                    if not first:
                        act.wait_ge(y_made, CHUNKS * TILES * n)
                nc.scalar.activation(x1h[:, columns(tiles)], l0[:, columns(tiles)], ACT.Identity,
                                     bias=b0c[:, 0:1]).then_inc(x1h_made, 1)

            def layer2_out(tile, to):
                act.wait_ge(gp_made, layer2_ready(tile))
                nc.scalar.copy(gram[:, :, bass.ds(to, TILE_B)], gp[:].rearrange("p (f b) -> p f b", f=F))
                nc.scalar.copy(sums1[:, bass.ds(tile * TILE_B, TILE_B)], s1[:, 0:TILE_B]).then_inc(gp_used, 1)

            def quarter_out(q):
                act.wait_ge(l2_made, q)
                nc.scalar.activation(sums2[:, bass.ds(q * QB, QB)], l2, ACT.Identity,
                                     bias=b2d[:, 0:1]).then_inc(l2_used, 1)

            def w2_out(c):
                act.wait_ge(w2_turned, c + 1)
                nc.scalar.copy(w2t[:, CF * c:CF * c + CF, :], (gp, s1)[c % 2][:].rearrange("p (f o) -> p f o", o=O)) \
                    .then_inc(w2_kept, 1)

            def body(n, kind):
                act.wait_ge(x0t_made, 2 * n + 1)
                for e in range(TILES * CHUNKS):
                    j, c = divmod(e, CHUNKS)
                    tile = n * TILES + j
                    if e == 1 and kind != "first":
                        upper(n, LAST, False)
                    if e == 7 and kind != "first":
                        fields(n, LAST, False)
                    if e == CHUNKS * (TILES - 1):
                        act.wait_ge(x0t_made, 2 * n + 2)
                    if c in HELPED:
                        multiply(tile, j, c)
                    if kind == "first" and W2_AT <= e - 1 < W2_AT + CHUNKS:
                        w2_out(e - 1 - W2_AT)
                    if c == LAYER2_AT + 1 and (kind != "first" or j > 0):
                        before = (n * TILES + (j - 1) + QG * TILES) % (QG * TILES) if kind != "first" else j - 1
                        layer2_out(tile - 1, before * TILE_B)
                    if e == QUARTER_AT[-1] + 1 and kind == "inner":
                        with act.If_eq(act.to_reg(n % QG), 0):
                            quarter_out(n // QG)
                    if e + PARTS_BEFORE in AHEAD_AT and kind != "last":
                        upper_product(n + 1, AHEAD_AT.index(e + PARTS_BEFORE))
                    if e == SPLIT_AT and kind != "last":
                        upper(n + 1, FIRST, False)
                        fields(n + 1, FIRST, False)

            def multiply(tile, j, c):
                h = HELPED.index(c)
                act.wait_ge(y_made, CHUNKS * tile + c + 1)
                before = (h - HSLOTS) % HN
                act.wait_ge(pool_step, pool_at(tile, max(before, 1) - (POOL_STEPS if h < HSLOTS else 0)))
                for k in range(CF):
                    f = CF * c + k
                    last = nc.scalar.activation(prod[:, h % HSLOTS, k, :], y[c % YB][:, k * O:(k + 1) * O],
                                                ACT.Copy, scale=x0t[:, j, f:f + 1])
                last.then_inc(prod_made, 1)

            act.wait_ge(bias_loaded, 48)
            for k, (what, r, bank) in enumerate(PREP):
                if what == "w1" and r == 0:
                    load(w2raw, w2, w2_loaded)
                    for t in range(ZT):
                        upper_product(0, t)
                    for tiles in (FIRST, LAST):
                        fields(0, tiles, True)
                        upper(0, tiles, True)
                act.wait_ge(prep_made, k + 1)
                part, of = weights(w0h, w1h, what, r, bank)
                nc.scalar.copy(part, of).then_inc(wh_made, 1)

            act.wait_ge(bias_made, 1)
            groups(act, body)
            layer2_out(GROUPS * TILES - 1, (QG * TILES - 1) * TILE_B)
            quarter_out(QUARTERS)
            for r in range(0, B // P, 2):
                act.wait_ge(turned, r + 1)
                nc.scalar.copy(outs[:, r, :], y[r][:, 0:L * O]).then_inc(outs_made[0], 1)

        @block.vector
        def _(dve):
            dve.sem_inc(acc_step, SN)

            dve.wait_ge(w0_loaded, 16)
            for s in range(F // 2 + 1):
                to = s * F
                if s == 0:
                    nc.vector.tensor_copy(w0pair[:, 0:F], w0raw[:, 0:F * F:F + 1])
                    continue
                whole = F - s if s < F // 2 else ZLAST
                a = w0raw[:, s:s + (whole - 1) * (F + 1) + 1:F + 1]
                b = w0raw[:, s * F:s * F + (whole - 1) * (F + 1) + 1:F + 1]
                last = nc.vector.tensor_tensor(w0pair[:, to:to + whole], a, b, ALU.add)
                if s < F // 2:
                    r = F - s
                    a = w0raw[:, r * F:r * F + (s - 1) * (F + 1) + 1:F + 1]
                    b = w0raw[:, r:r + (s - 1) * (F + 1) + 1:F + 1]
                    last = nc.vector.tensor_tensor(w0pair[:, to + r:to + F], a, b, ALU.add)
            last.then_inc(pair_made, 1)
            dve.wait_ge(bias_loaded, 48)
            nc.vector.tensor_scalar(b0d[:], b0c[:], float(D), None, ALU.mult)
            nc.vector.tensor_scalar(b2d[:], b2c[:], float(D), None, ALU.mult).then_inc(bias_made, 1)

            def lower_product(n, t):
                rows, slot = z_rows(t), t % ZPARTS
                dve.wait_ge(zh_made, ZT * n + t + 1)
                nc.vector.tensor_tensor(zl[0:rows, slot, :], z[0:rows, zslot(t), :],
                                        zh[0:rows, slot, :].bitcast(F32), ALU.subtract).then_inc(zl_made, 1)

            def own_rows(tile, j):
                dve.wait_ge(gp_made, layer2_ready(tile - 2))
                shape = [P, F, TILE_B]
                nc.vector.tensor_tensor(bd[:, j % 2], x0t[:, j, :].unsqueeze(2).to_broadcast(shape),
                                        own[:].unsqueeze(1).to_broadcast(shape), ALU.mult).then_inc(bd_made, 1)

            def lower(n, tiles):
                dve.wait_ge(x1h_made, 2 * n + (1 if tiles == FIRST else 2))
                cols = columns(tiles)
                nc.vector.scalar_tensor_tensor(out=x1l[:, cols], in0=l0[:, cols], scalar=b0c[:, 0:1],
                                               in1=x1h[:, cols].bitcast(F32), op0=ALU.add,
                                               op1=ALU.subtract).then_inc(x1l_made, 1)

            def sum_elements(n):
                to = sums0[:, bass.ds(n * GROUP_B, GROUP_B)]
                nc.vector.tensor_reduce(to, l0[:].rearrange("p (b d) -> p b d", d=D), AX.X,
                                        ALU.add).then_inc(l0_used, 1)

            def add_fields(tile, j, c):
                m = SUMMED.index(c)
                if m == 0:
                    dve.wait_ge(x2_made, x2_ready(tile - 2))
                dve.wait_ge(y_made, CHUNKS * tile + c + 1)
                for k in range(CF):
                    f = CF * c + k
                    to, of = acc[:, j % 2, k, :], y[c % YB][:, k * O:(k + 1) * O]
                    if m > 0 and k % 2 == 0:
                        dve.wait_ge(acc_step, SN * tile + (SN + CF * (m - 1) + k + 2))
                    if m == 0 and k > 0:
                        ins = nc.vector.tensor_scalar(to, of, x0t[:, j, f:f + 1], None, ALU.mult)
                    else:
                        ins = nc.vector.scalar_tensor_tensor(out=to, in0=of, scalar=x0t[:, j, f:f + 1],
                                                             in1=b1r[:] if m == 0 else to,
                                                             op0=ALU.mult, op1=ALU.add)
                    ins.then_inc(acc_step, 1)

            def body(n, kind):
                dve.wait_ge(x0t_made, 2 * n + 1)
                for e in range(TILES * CHUNKS):
                    j, c = divmod(e, CHUNKS)
                    if e == 2 and kind != "first":
                        lower(n, LAST)
                        sum_elements(n)
                    if e == CHUNKS * (TILES - 1):
                        dve.wait_ge(x0t_made, 2 * n + 2)
                    if c in SUMMED:
                        add_fields(n * TILES + j, j, c)
                    if c == 5:
                        own_rows(n * TILES + j, j)
                    if e + PARTS_BEFORE in AHEAD_AT and kind != "last":
                        lower_product(n + 1, AHEAD_AT.index(e + PARTS_BEFORE))
                    if e == SPLIT_AT and kind != "last":
                        lower(n + 1, FIRST)

            dve.wait_ge(consts_made, 1)
            for k, (what, r, bank) in enumerate(PREP):
                if (what, r) == ("w1", 0):
                    for t in range(ZT):
                        lower_product(0, t)
                    lower(0, FIRST)
                    lower(0, LAST)
                    sum_elements(0)
                dve.wait_ge(wh_made, k + 1)
                part, of = weights(w0l, w1l, what, r, bank)
                whole, _ = weights(w0h, w1h, what, r, bank)
                nc.vector.tensor_tensor(part, of, whole.bitcast(F32), ALU.subtract).then_inc(y_used[bank], 1)
            groups(dve, body)
            dve.wait_ge(l0_used, GROUPS)
            nc.vector.tensor_scalar(sums0[:, 0:B], sums0[:, 0:B], b0d[:, 0:1], None, ALU.add).then_inc(sums_made, 1)
            for r in range(1, B // P, 2):
                dve.wait_ge(turned, r + 1)
                nc.vector.tensor_copy(outs[:, r, :], y[r][:, 0:L * O]).then_inc(outs_made[1], 1)

        @block.tensor
        def _(pe):
            pe.sem_inc(gp_made, 2)

            def by_parts(to, xh, xl, wh, wl, first, last, x_stationary):
                for k, (a, b) in enumerate(((xh, wh), (xh, wl), (xl, wh))):
                    stationary, moving = (a, b) if x_stationary else (b, a)
                    ins = nc.tensor.matmul(to, stationary, moving, start=(first and k == 0), stop=(last and k == 2))
                return ins

            def layer0(n, t):
                rows, slot = z_rows(t), t % ZPARTS
                pe.wait_ge(zl_made, ZT * n + t + 1)
                by_parts(l0[:], zh[0:rows, slot, :], zl[0:rows, slot, :], w0h[0:rows, t, :], w0l[0:rows, t, :],
                         t == 0, t == ZT - 1, False).then_inc(z_used, 1)

            def turn_fields():
                for j in range(TILES):
                    last = nc.tensor.transpose(xt[:, j, :], xg[0:F, j * P:(j + 1) * P], ident[0:F, 0:F])
                last.then_inc(xt_made, 1)

            def turn_w2(c):
                if c >= 2:
                    pe.wait_ge(w2_kept, c - 1)
                for k in range(CF):
                    last = nc.tensor.transpose((gp, s1)[c % 2][:, k * O:(k + 1) * O],
                                               w2raw.rearrange("o (h f) -> o f h", f=F)[:, CF * c + k, :], ident[:])
                last.then_inc(w2_turned, 1)

            def quarter(q, part, fields_kept):
                if part == 0:
                    pe.wait_ge(gp_used, q * (QG * TILES) + 1)
                    pe.wait_ge(x0t_made, fields_kept)
                each = F // QUARTER_PARTS
                for f in range(part * each, (part + 1) * each):
                    last = nc.tensor.matmul(l2, w2t[:, f, :], gram[:, f, :], start=(f == 0), stop=(f == F - 1))
                if part == QUARTER_PARTS - 1:
                    last.then_inc(l2_made, 1)

            def layer2(tile, slot):
                pe.wait_ge(x2_made, x2_ready(tile))
                pe.wait_ge(bd_made, tile + 1)
                pe.wait_ge(gp_used, tile + 1)
                nc.tensor.matmul(gp[:], x2[:, slot], bd[:, slot].rearrange("p f b -> p (f b)"), start=True, stop=True)
                nc.tensor.matmul(s1[:, 0:TILE_B], x2[:, slot], own[:], start=True, stop=True).then_inc(gp_made, 1)

            def chunk(tile, j, c):
                before, late = (c - YB) % CHUNKS, c < YB
                if before in HELPED:
                    value = HN * tile + (HN + HELPED.index(before) + 1) - (HN if late else 0)
                    pe.wait_ge(prod_made, value)
                else:
                    value = SN * tile + (SN + CF * SUMMED.index(before) + CF) - (SN if late else 0)
                    pe.wait_ge(acc_step, value)
                cols = slice(j * P, (j + 1) * P)
                by_parts(y[c % YB][:], x1h[:, cols], x1l[:, cols], w1h[:, c, :], w1l[:, c, :],
                         True, True, True).then_inc(y_made, 1)

            pe.wait_ge(consts_made, 1)
            for k, (what, r, bank) in enumerate(PREP):
                if (what, r) == ("w0", 0):
                    pe.wait_ge(pair_made, 1)
                if (what, r) == ("w1", 0):
                    for i in range(YB):
                        pe.wait_ge(y_used[i], uses(PREP[:k], i))
                    for t in range(ZT):
                        layer0(0, t)
                    turn_fields()
                    pe.wait_ge(w1_loaded, 16 * 8)
                if uses(PREP[:k], bank):
                    pe.wait_ge(y_used[bank], uses(PREP[:k], bank))
                if what == "w0":
                    for t in range(4 * r, min(4 * r + 4, ZT)):
                        rows = z_rows(t)
                        last = nc.tensor.transpose(y[bank][0:rows, (t % 4) * O:(t % 4 + 1) * O],
                                                   w0pair[:, t * P:t * P + rows], ident[:])
                else:
                    raw = w1raw.rearrange("o (h f) -> o f h", f=F)
                    for k4 in range(CF):
                        last = nc.tensor.transpose(y[bank][:, k4 * O:(k4 + 1) * O], raw[:, CF * r + k4, :], ident[:])
                last.then_inc(prep_made, 1)
            for i in range(YB):
                pe.wait_ge(y_used[i], uses(PREP, i))

            def body(n, kind):
                for e in range(TILES * CHUNKS):
                    j, c = divmod(e, CHUNKS)
                    tile = n * TILES + j
                    if c == 0 and j in (0, TILES - 1):
                        pe.wait_ge(x1h_made, 2 * n + (2 if j else 1))
                        pe.wait_ge(x1l_made, 2 * n + (2 if j else 1))
                    if e == TURN_AT and kind != "last":
                        pe.wait_ge(x0t_made, 2 * n + 2)
                        pe.wait_ge(l2_used, (n // QG if kind == "inner" else 0) + 1)
                    chunk(tile, j, c)
                    if kind == "first" and W2_AT <= e < W2_AT + CHUNKS:
                        if e == W2_AT:
                            pe.wait_ge(w2_loaded, 16 * 8)
                        turn_w2(e - W2_AT)
                    if c == LAYER2_AT and (kind != "first" or j > 0):
                        if kind == "first" and j == 1:
                            pe.wait_ge(w2_kept, CHUNKS)
                        layer2(tile - 1, (j - 1) % 2)
                    if e in QUARTER_AT and kind == "inner":
                        with pe.If_eq(pe.to_reg(n % QG), 0):
                            quarter(n // QG, QUARTER_AT.index(e), 2 * n + 2)
                    if kind != "last":
                        if e == AHEAD_AT[0]:
                            pe.wait_ge(l0_used, n + 1)
                        if e in AHEAD_AT:
                            layer0(n + 1, AHEAD_AT.index(e))
                        if e == TURN_AT:
                            turn_fields()

            groups(pe, body)
            layer2(GROUPS * TILES - 1, 1)
            for part in range(QUARTER_PARTS):
                quarter(QUARTERS, part, 2 * GROUPS)

            pe.wait_ge(sums_made, 1)
            pe.wait_ge(l2_used, QUARTERS + 1)
            for r in range(B // P):
                for k, sums in enumerate((sums0[:], sums1[:], sums2[:, QB:QB + B])):
                    last = nc.tensor.transpose(y[r][:, k * O:(k + 1) * O], sums[:, r * P:(r + 1) * P], ident[:])
                last.then_inc(turned, 1)


_INS = ["r_input", "L0_rec_W0", "L0_rec_b0", "L0_rec_W1", "L0_rec_b1", "L0_rec_W2", "L0_rec_b2"]
_OUTS = [((B, L * O), "float32")]


def kernel(**inputs):
    import numpy as _np
    import concourse.bacc as _bacc
    from concourse import mybir as _mybir
    from concourse.bass_utils import run_bass_kernel_spmd as _run

    nc = _bacc.Bacc("TRN2", target_bir_lowering=False, num_devices=1)
    arrays, args = {}, []
    for name in _INS:
        a = _np.ascontiguousarray(inputs[name])
        arrays[f"in_{name}_dram"] = a
        args.append(nc.dram_tensor(f"in_{name}_dram", a.shape, _mybir.dt.from_np(a.dtype), kind="ExternalInput").ap())
    for i, (shape, dtype) in enumerate(_OUTS):
        dt = _mybir.dt.from_np(_np.dtype(dtype))
        args.append(nc.dram_tensor(f"out_{i}_dram", shape, dt, kind="ExternalOutput").ap())
    cin_kernel(nc, *args)
    r = _run(nc, [arrays], core_ids=[0])
    got = tuple(r.results[0][f"out_{i}_dram"] for i in range(len(_OUTS)))
    return got[0]
```

```python
from contextlib import ExitStack

import concourse.bass as bass
from concourse import mybir

F32 = mybir.dt.float32
F32R = mybir.dt.float32r
ALU = mybir.AluOpType
ACT = mybir.ActivationFunctionType
AX = mybir.AxisListType

B, F, D = 512, 64, 16
O = 128
P = 128
L = 3

TILE_B = P // D
HALF = P // 2
HALF_B = TILE_B // 2
TILES = 4
GROUP = TILES * P
GROUP_B = TILES * TILE_B
GROUPS = B // GROUP_B
QUARTERS = 4
QG = GROUPS // QUARTERS
QB = B // QUARTERS

ZT = F // 4 + 1
ZLAST = F // 2
ZCOPIES = 3
UPPER_LOWER, LOWER_UPPER = slice(ZLAST, 2 * ZLAST), slice(2 * ZLAST, 3 * ZLAST)
ZSLOTS = 6
ZPARTS = 4

CF = 4
CHUNK = CF * O
CHUNKS = F // CF
YB = 4
HELPED = (1, 4, 6, 9, 12, 14)
HN = len(HELPED)
SUMMED = tuple(c for c in range(CHUNKS) if c not in HELPED)
SN = CF * len(SUMMED)
HSLOTS = 3
POOL_STEPS = HN + 1

X2H_AT, X2L_AT = 8, 10
LAYER2_AT = 14
OWN_AT = 11
BDL_AT = (11, 13, 15, 15)
QUARTER_PARTS = 8
QUARTER_AT = [CHUNKS + 2 + k for k in range(QUARTER_PARTS)]
LOWER_AT = 4
SUM_AT = 6
FIELDS_LOWER_AT = (9, 14)
AHEAD_AT = [9 + t * 46 // (ZT - 1) for t in range(ZT)]
PARTS_BEFORE = 5
LOWER_BEFORE = 4
TURN_AT = 30
SPLIT_AT = AHEAD_AT[-1] + 1
LOWER_AFTER = 3
W2_AT = 10
W1_LEAD = 3
W2_LOADED_AT = 13
POOL_PAIRS = 17
PRODUCTS_AT = ((2, 1, 1, 1, 1, 0), (1, 1, 1, 1, 1, 0), (1, 1, 1, 1, 1, 0), (1, 0, 0, 0, 0, 0))


def zslot(t):
    return t % ZSLOTS


def last_in(t, slots):
    return max(range(t % slots, ZT, slots))


def cin_kernel(nc, x, w0, b0, w1, b1, w2, b2, out):
    with ExitStack() as ctx:
        def sb(name, shape, dt=F32):
            return ctx.enter_context(nc.sbuf_tensor(name, shape, dt))

        def ps(name, shape):
            return ctx.enter_context(nc.psum_tensor(name, shape, F32))

        def sem(name):
            return ctx.enter_context(nc.semaphore(name))

        w1h = sb("w1h", [P, CHUNKS, CHUNK], F32R)
        w1l = sb("w1l", [P, CHUNKS, CHUNK], F32R)
        w2t = sb("w2t", [P, F, O])
        gram = sb("gram", [P, F, QB])
        w0h = sb("w0h", [P, ZT, O], F32R)
        w0l = sb("w0l", [P, ZT - 1, O], F32R)
        z = sb("z", [P, ZSLOTS, GROUP])
        zh = sb("zh", [P, ZPARTS, GROUP], F32R)
        zl = sb("zl", [P, ZPARTS, GROUP], F32R)
        xg = sb("xg", [P, GROUP])
        x1h = sb("x1h", [P, GROUP], F32R)
        x1l = sb("x1l", [P, GROUP], F32R)
        x0t = sb("x0t", [P, TILES, F])
        x0th = sb("x0th", [P, TILES, F], F32R)
        x0tl = sb("x0tl", [P, TILES, F])
        bdh = sb("bdh", [P, 2, HALF_B, F], F32R)
        bdl = sb("bdl", [P, 2, HALF_B, F], F32R)
        acc = sb("acc", [P, 2, CF, O])
        prod = sb("prod", [P, HSLOTS, CF, O])
        pacc = sb("pacc", [P, CF, O])
        x2 = sb("x2", [P, 2, O])
        x2h = sb("x2h", [P, 2, O], F32R)
        x2l = sb("x2l", [P, 2, O], F32R)
        own_r = sb("own_r", [P, TILE_B], F32R)
        ident = sb("ident", [P, P])
        own = sb("own", [P, TILE_B])
        own_half = sb("own_half", [P, HALF_B])
        b0c = sb("b0c", [P, 1])
        b2c = sb("b2c", [P, 1])
        b0d = sb("b0d", [P, 1])
        b2d = sb("b2d", [P, 1])
        b1r = sb("b1r", [P, O])
        sums = sb("sums", [P, L, B])

        sums0, sums1 = sums[:, 0], sums[:, 1]
        sums2_from_1 = sums[:].rearrange("p l b -> p (l b)")[:, 2 * B - QB:]

        w1raw = w2t[:].rearrange("p f o -> p (f o)")
        w2raw = gram[:].rearrange("p f b -> p (f b)")
        w0raw = w2raw[:, 0:F * F]
        w0pair = w2raw[:, F * F:F * F + ZT * P]
        outs = z[:].rearrange("p t n -> p (t n)")[:, 0:(B // P) * L * O].rearrange(
            "p (r n) -> p r n", r=B // P)

        y = [ps(f"y{i}", [P, CHUNK]) for i in range(YB)]
        l0 = ps("l0", [P, GROUP])
        l2p = ps("l2p", [P, 2, CHUNK])
        xt = ps("xt", [P, TILES, F])
        s1 = l2p[:, 1, HALF_B * F:HALF_B * F + TILE_B]
        l2 = xt[:].rearrange("p t f -> p (t f)")[:, 0:QB]

        w0_loaded = sem("w0_loaded")
        w1_loaded = sem("w1_loaded")
        w2_loaded = sem("w2_loaded")
        bias_loaded = sem("bias_loaded")
        ones_set = sem("ones_set")
        consts_made = sem("consts_made")
        pair_made = sem("pair_made")
        far_pair_made = sem("far_pair_made")
        bias_made = sem("bias_made")
        prep_made = sem("prep_made")
        wh_made = sem("wh_made")
        w2_turned = sem("w2_turned")
        w2_kept = sem("w2_kept")
        xg_loaded = sem("xg_loaded")
        b_loaded = [sem(f"b_loaded{i}") for i in range(ZSLOTS)]
        z_made = sem("z_made")
        zh_made = sem("zh_made")
        zl_made = sem("zl_made")
        z_used = sem("z_used")
        xt_made = sem("xt_made")
        x0t_made = sem("x0t_made")
        own_made = sem("own_made")
        x0tl_made = sem("x0tl_made")
        bdh_made = sem("bdh_made")
        bdl_made = sem("bdl_made")
        x2h_made = sem("x2h_made")
        x2l_made = sem("x2l_made")
        x1h_made = sem("x1h_made")
        x1l_made = sem("x1l_made")
        l0_used = sem("l0_used")
        y_made = sem("y_made")
        y_used = [sem(f"y_used{i}") for i in range(YB)]
        acc_step = sem("acc_step")
        prod_made = sem("prod_made")
        pool_step = sem("pool_step")
        x2_made = sem("x2_made")
        l2p_made = sem("l2p_made")
        l2p_used = sem("l2p_used")
        l2_made = sem("l2_made")
        l2_used = sem("l2_used")
        sums_made = sem("sums_made")
        turned = sem("turned")
        outs_made = [sem("outs_made0"), sem("outs_made1")]
        stored = sem("stored")

        W0_STEPS = -(-ZT // 4)
        def steps_before(lead):
            steps = [("w0", r, r % YB) for r in range(W0_STEPS)]
            for i in range(CHUNKS + lead):
                if i < CHUNKS:
                    steps.append(("w1", i, i % YB))
                steps += [("l0", t, None) for t in range(ZT) if t * CHUNKS // ZT == i - lead]
            return steps

        PREP, PE_PREP = steps_before(0), steps_before(W1_LEAD)

        def turned_in(steps):
            return sum(what != "l0" for what, _, _ in steps)

        def uses(steps, bank):
            return sum(b == bank for _, _, b in steps)

        def weights(of_w0, of_w1, what, r, bank):
            if what == "w1":
                return of_w1[:, r, :], y[bank][:]
            if r < W0_STEPS - 1:
                return of_w0[:, 4 * r:4 * r + 4, :], y[bank][:].rearrange("p (t o) -> p t o", o=O)
            rows = slice(0, z_rows(ZT - 1)) if of_w0 is w0h else UPPER_LOWER
            return w0h[rows, ZT - 1, :], y[bank][rows, 0:O]

        def z_rows(t):
            return P if t < ZT - 1 else ZCOPIES * ZLAST

        def tile_added(tile):
            return SN * tile + 2 * SN

        def x2_ready(tile):
            return tile + 3

        def layer2_ready(tile):
            return tile + 3

        def pool_at(tile, step):
            return POOL_STEPS * tile + (POOL_STEPS + 1 + step)

        FIRST, LAST = slice(0, TILES - 1), slice(TILES - 1, TILES)

        def columns(tiles):
            return slice(tiles.start * P, tiles.stop * P)

        def groups(engine, body):
            body(0, "first")
            with engine.Fori(1, GROUPS - 1) as n:
                body(n, "inner")
            body(GROUPS - 1, "last")

        block = ctx.enter_context(nc.Block())

        @block.sync
        def _(sp):
            def front(n, first):
                if first:
                    rows = x[0:GROUP_B]
                else:
                    rows = x[bass.ds(n * GROUP_B, GROUP_B), :, :]
                    sp.wait_ge(z_made, ZT * n)
                    sp.wait_ge(xt_made, n)
                for half in range(2):
                    sp.dma_start(xg[half * F:(half + 1) * F, :].rearrange("f (b d) -> f b d", d=D),
                                 rows.rearrange("b f d -> f b d")).then_inc(xg_loaded, 16)
                sp.wait_ge(xg_loaded, 32 * n + 32)
                for t in range(ZT):
                    if t >= ZSLOTS:
                        sp.wait_ge(zl_made, ZT * n + (t - ZSLOTS + 1))
                    elif not first:
                        sp.wait_ge(zl_made, ZT * (n - 1) + (last_in(t, ZSLOTS) + 1))
                    shift, slot = 2 * t, zslot(t)
                    if t < ZT - 1:
                        for half in range(2):
                            sp.dma_start(z[half * F:(half + 1) * F, slot, :],
                                         xg[shift + half:shift + half + F, :]).then_inc(b_loaded[slot], 16)
                    else:
                        rows = z_rows(t)
                        sp.dma_start(z[0:rows, slot, :], xg[shift:shift + rows, :]).then_inc(b_loaded[slot], 32)

            front(0, True)
            with sp.Fori(1, GROUPS) as n:
                front(n, False)
            for r in range(B // P):
                sp.wait_ge(outs_made[r % 2], r // 2 + 1)
                sp.dma_start(out[r * P:(r + 1) * P, :], outs[:, r, :]).then_inc(stored, 16)
            sp.wait_ge(stored, 16 * (B // P))

        def pair_weights(tensor_tensor, shifts):
            for s in shifts:
                to = s * F
                whole = F - s if s < F // 2 else ZLAST
                a = w0raw[:, s:s + (whole - 1) * (F + 1) + 1:F + 1]
                b = w0raw[:, s * F:s * F + (whole - 1) * (F + 1) + 1:F + 1]
                for copy in range(1 if s < F // 2 else ZCOPIES):
                    last = tensor_tensor(w0pair[:, to + copy * ZLAST:to + copy * ZLAST + whole], a, b, ALU.add)
                if s < F // 2:
                    r = F - s
                    a = w0raw[:, r * F:r * F + (s - 1) * (F + 1) + 1:F + 1]
                    b = w0raw[:, r:r + (s - 1) * (F + 1) + 1:F + 1]
                    last = tensor_tensor(w0pair[:, to + r:to + F], a, b, ALU.add)
            return last

        @block.gpsimd
        def _(pool):
            pool.sem_inc(pool_step, POOL_STEPS + 1)
            pool.sem_inc(x2_made, 2)
            nc.gpsimd.memset(ident[:], 0.0)
            nc.gpsimd.memset(own[:], 1.0).then_inc(ones_set, 1)
            pool.wait_ge(ones_set, 1)
            nc.gpsimd.affine_select(out=ident[:], in_=ident[:], compare_op=ALU.not_equal, fill=1.0, base=0,
                                    pattern=[[-1, P]], channel_multiplier=1).then_inc(ones_set, 1)
            nc.gpsimd.affine_select(out=own[:], in_=own[:], compare_op=ALU.is_ge, fill=0.0, base=0,
                                    pattern=[[-D, TILE_B]], channel_multiplier=1).then_inc(ones_set, 1)
            pool.wait_ge(ones_set, 3)
            nc.gpsimd.affine_select(out=own[:], in_=own[:], compare_op=ALU.is_ge, fill=0.0, base=D - 1,
                                    pattern=[[D, TILE_B]], channel_multiplier=-1).then_inc(consts_made, 1)

            def product(n, t):
                slot, rows = zslot(t), z_rows(t)
                of_group = len(range(slot, ZT, ZSLOTS))
                pool.wait_ge(b_loaded[slot], 32 * (of_group * n + t // ZSLOTS + 1))
                nc.gpsimd.tensor_tensor(z[0:rows, slot, :], z[0:rows, slot, :], xg[0:rows, :],
                                        ALU.mult).then_inc(z_made, 1)

            def add_products(tile, h):
                pool.wait_ge(prod_made, HN * tile + (HN + h + 1))
                pool.wait_ge(pool_step, pool_at(tile, h - 1))
                if h == 1:
                    pool.wait_ge(x2_made, x2_ready(tile - 1))
                    nc.gpsimd.tensor_tensor(pacc[:], prod[:, 0], prod[:, 1], ALU.add).then_inc(pool_step, 1)
                else:
                    nc.gpsimd.tensor_tensor(pacc[:], pacc[:], prod[:, h % HSLOTS], ALU.add).then_inc(pool_step, 1)

            def combine(tile, slot):
                pool.wait_ge(acc_step, tile_added(tile))
                pool.wait_ge(pool_step, pool_at(tile, HN - 1))
                nc.gpsimd.tensor_tensor(pacc[:], pacc[:], acc[:, slot], ALU.add).then_inc(pool_step, 1)
                pool.wait_ge(pool_step, pool_at(tile, HN))
                nc.gpsimd.tensor_tensor(pacc[:, 0:2], pacc[:, 0:2], pacc[:, 2:4], ALU.add).then_inc(pool_step, 1)
                pool.wait_ge(pool_step, pool_at(tile, HN + 1))
                pool.wait_ge(l2p_made, layer2_ready(tile - 2))
                nc.gpsimd.tensor_tensor(x2[:, slot], pacc[:, 0], pacc[:, 1], ALU.add).then_inc(x2_made, 1)

            def body(n, kind):
                ahead = iter(range(ZT))
                for j in range(TILES):
                    tile = n * TILES + j

                    def products(step):
                        if kind != "last":
                            for _ in range(PRODUCTS_AT[j][step]):
                                product(n + 1, next(ahead))

                    products(0)
                    if kind != "first" or j > 0:
                        combine(tile - 1, (j - 1) % 2)
                    for h in range(1, HN):
                        products(h)
                        add_products(tile, h)

            pool.wait_ge(w0_loaded, 16)
            pair_weights(nc.gpsimd.tensor_tensor, range(POOL_PAIRS, F // 2 + 1)).then_inc(far_pair_made, 1)
            for t in range(ZT):
                product(0, t)
            groups(pool, body)
            combine(GROUPS * TILES - 1, 1)

        @block.scalar
        def _(act):
            act.sem_inc(l2p_used, 1)
            act.sem_inc(l2_used, 1)
            act.sem_inc(prod_made, HN)

            def load(to, of, loaded):
                part = F * O // 8
                for k in range(8):
                    act.dma_start(to[:, k * part:(k + 1) * part], of[:, k * part:(k + 1) * part]).then_inc(loaded, 16)

            act.dma_start(w0raw, w0).then_inc(w0_loaded, 16)
            act.dma_start(b0c[:], b0.rearrange("(p a) -> p a", a=1)).then_inc(bias_loaded, 16)
            act.dma_start(b2c[:], b2.rearrange("(p a) -> p a", a=1)).then_inc(bias_loaded, 16)
            act.dma_start(b1r[:], b1.rearrange("(a o) -> a o", a=1).to_broadcast((P, O))).then_inc(bias_loaded, 16)
            load(w1raw, w1, w1_loaded)

            def upper_product(n, t):
                rows = z_rows(t)
                act.wait_ge(z_made, ZT * n + t + 1)
                if t >= ZPARTS:
                    act.wait_ge(z_used, ZT * n + (t - ZPARTS + 1))
                elif not isinstance(n, int) or n > 0:
                    act.wait_ge(z_used, ZT * (n - 1) + (last_in(t, ZPARTS) + 1))
                nc.scalar.copy(zh[0:rows, t % ZPARTS, :], z[0:rows, zslot(t), :]).then_inc(zh_made, 1)

            def fields(n, tiles, first):
                act.wait_ge(xt_made, n + 1)
                if not first:
                    act.wait_ge(acc_step, tile_added((n - 1) * TILES + (tiles.stop - 1)))
                    act.wait_ge(prod_made, HN * TILES * n - HN * TILES + HN * (tiles.stop + 1))
                    act.wait_ge(x0tl_made, 2 * n + (1 if tiles == LAST else 0) - 1)
                nc.scalar.copy(x0th[:, tiles, :], xt[:, tiles, :])
                nc.scalar.copy(x0t[:, tiles, :], xt[:, tiles, :]).then_inc(x0t_made, 1)

            def upper(n, tiles, first):
                if tiles == FIRST:
                    act.wait_ge(z_used, ZT * n + ZT)
                else:
                    act.wait_ge(x1l_made, 2 * n + 1)
                    if not first:
                        act.wait_ge(y_made, CHUNKS * TILES * n)
                nc.scalar.activation(x1h[:, columns(tiles)], l0[:, columns(tiles)], ACT.Identity,
                                     bias=b0c[:, 0:1]).then_inc(x1h_made, 1)

            def upper_x2(tile, slot):
                act.wait_ge(x2_made, x2_ready(tile))
                nc.scalar.copy(x2h[:, slot], x2[:, slot]).then_inc(x2h_made, 1)

            def lower_row(tile, n, j, b):
                if b == 0:
                    act.wait_ge(x0tl_made, 2 * n + (2 if j == TILES - 1 else 1))
                    act.wait_ge(l2p_made, layer2_ready(tile - 2))
                    act.wait_ge(own_made, 1)
                ins = nc.scalar.activation(bdl[:, j % 2, b, :], x0tl[:, j, :], ACT.Copy, scale=own_half[:, b:b + 1])
                if b == HALF_B - 1:
                    ins.then_inc(bdl_made, 1)

            def layer2_out(tile, to):
                act.wait_ge(l2p_made, layer2_ready(tile))
                nc.scalar.copy(gram[:, :, bass.ds(to, TILE_B)].rearrange("p f (k b) -> p f k b", k=2),
                               l2p[:, :, 0:HALF_B * F].rearrange("p k (b f) -> p f k b", f=F))
                nc.scalar.copy(sums1[:, bass.ds(tile * TILE_B, TILE_B)], s1).then_inc(l2p_used, 1)

            def quarter_out(q):
                act.wait_ge(l2_made, q)
                nc.scalar.activation(sums2_from_1[:, bass.ds(q * QB, QB)], l2, ACT.Identity,
                                     bias=b2d[:, 0:1]).then_inc(l2_used, 1)

            def w2_out(c):
                act.wait_ge(w2_turned, c + 1)
                nc.scalar.copy(w2t[:, CF * c:CF * c + CF, :], l2p[:, c % 2, :].rearrange("p (f o) -> p f o", o=O)) \
                    .then_inc(w2_kept, 1)

            def body(n, kind):
                act.wait_ge(x0t_made, 2 * n + 1)
                for e in range(TILES * CHUNKS):
                    j, c = divmod(e, CHUNKS)
                    tile = n * TILES + j
                    if e == 1 and kind != "first":
                        upper(n, LAST, False)
                    if e == 7 and kind != "first":
                        fields(n, LAST, False)
                    if e == CHUNKS * (TILES - 1):
                        act.wait_ge(x0t_made, 2 * n + 2)
                    if c in HELPED:
                        multiply(tile, j, c)
                    if kind == "first" and W2_AT <= e - 1 < W2_AT + CHUNKS:
                        w2_out(e - 1 - W2_AT)
                    if c == X2H_AT and (kind != "first" or j > 0):
                        upper_x2(tile - 1, (j - 1) % 2)
                    for b, at in enumerate(BDL_AT):
                        if at == c:
                            lower_row(tile, n, j, b)
                    if c == LAYER2_AT + 1 and (kind != "first" or j > 0):
                        before = (n * TILES + (j - 1) + QG * TILES) % (QG * TILES) if kind != "first" else j - 1
                        layer2_out(tile - 1, before * TILE_B)
                    if e == QUARTER_AT[-1] + 1 and kind == "inner":
                        with act.If_eq(act.to_reg(n % QG), 0):
                            quarter_out(n // QG)
                    if e + PARTS_BEFORE in AHEAD_AT and kind != "last":
                        upper_product(n + 1, AHEAD_AT.index(e + PARTS_BEFORE))
                    if e == SPLIT_AT and kind != "last":
                        upper(n + 1, FIRST, False)
                        fields(n + 1, FIRST, False)

            def multiply(tile, j, c):
                h = HELPED.index(c)
                act.wait_ge(y_made, CHUNKS * tile + c + 1)
                before = (h - HSLOTS) % HN
                act.wait_ge(pool_step, pool_at(tile, max(before, 1) - (POOL_STEPS if h < HSLOTS else 0)))
                for k in range(CF):
                    f = CF * c + k
                    last = nc.scalar.activation(prod[:, h % HSLOTS, k, :], y[c % YB][:, k * O:(k + 1) * O],
                                                ACT.Copy, scale=x0t[:, j, f:f + 1])
                last.then_inc(prod_made, 1)

            act.wait_ge(bias_loaded, 48)
            for k, (what, r, bank) in enumerate(PREP):
                if what == "l0":
                    upper_product(0, r)
                    continue
                if (what, r) == ("w1", W2_LOADED_AT):
                    load(w2raw, w2, w2_loaded)
                act.wait_ge(prep_made, turned_in(PREP[:k]) + 1)
                part, of = weights(w0h, w1h, what, r, bank)
                nc.scalar.copy(part, of).then_inc(wh_made, 1)

            for tiles in (FIRST, LAST):
                fields(0, tiles, True)
                upper(0, tiles, True)
            act.wait_ge(bias_made, 1)
            groups(act, body)
            upper_x2(GROUPS * TILES - 1, 1)
            layer2_out(GROUPS * TILES - 1, (QG * TILES - 1) * TILE_B)
            quarter_out(QUARTERS)
            for r in range(0, B // P, 2):
                act.wait_ge(turned, r + 1)
                nc.scalar.copy(outs[:, r, :], y[r][:, 0:L * O]).then_inc(outs_made[0], 1)

        @block.vector
        def _(dve):
            dve.sem_inc(acc_step, SN)

            dve.wait_ge(w0_loaded, 16)
            nc.vector.tensor_copy(w0pair[:, 0:F], w0raw[:, 0:F * F:F + 1])
            for r in range(W0_STEPS):
                shifts = range(max(8 * r, 1), min(8 * r + 8, POOL_PAIRS))
                if shifts:
                    pair_weights(nc.vector.tensor_tensor, shifts).then_inc(pair_made, 1)
            dve.wait_ge(bias_loaded, 48)
            nc.vector.tensor_scalar(b0d[:], b0c[:], float(D), None, ALU.mult)
            nc.vector.tensor_scalar(b2d[:], b2c[:], float(D), None, ALU.mult).then_inc(bias_made, 1)

            def lower_product(n, t):
                rows, slot = z_rows(t), t % ZPARTS
                dve.wait_ge(zh_made, ZT * n + t + 1)
                if t == ZT - 1:
                    part = zh[LOWER_UPPER, slot, :]
                    nc.vector.tensor_tensor(part, z[LOWER_UPPER, zslot(t), :], part.bitcast(F32),
                                            ALU.subtract).then_inc(zl_made, 1)
                    return
                nc.vector.tensor_tensor(zl[0:rows, slot, :], z[0:rows, zslot(t), :],
                                        zh[0:rows, slot, :].bitcast(F32), ALU.subtract).then_inc(zl_made, 1)

            def own_rows(tile, j):
                dve.wait_ge(l2p_made, layer2_ready(tile - 2))
                dve.wait_ge(own_made, 1)
                shape = [P, HALF_B, F]
                nc.vector.tensor_tensor(bdh[:, j % 2], x0th[:, j, :].bitcast(F32).unsqueeze(1).to_broadcast(shape),
                                        own_half[:].unsqueeze(2).to_broadcast(shape), ALU.mult).then_inc(bdh_made, 1)

            def lower_fields(n, tiles, first):
                dve.wait_ge(x0t_made, 2 * n + (1 if tiles == FIRST else 2))
                if not first:
                    dve.wait_ge(bdl_made, TILES * (n - 1) + tiles.stop)
                nc.vector.tensor_tensor(x0tl[:, tiles, :], x0t[:, tiles, :], x0th[:, tiles, :].bitcast(F32),
                                        ALU.subtract).then_inc(x0tl_made, 1)

            def lower_x2(tile, slot):
                dve.wait_ge(x2h_made, tile + 1)
                nc.vector.tensor_tensor(x2l[:, slot], x2[:, slot], x2h[:, slot].bitcast(F32),
                                        ALU.subtract).then_inc(x2l_made, 1)

            def lower(n, tiles):
                dve.wait_ge(x1h_made, 2 * n + (1 if tiles == FIRST else 2))
                cols = columns(tiles)
                nc.vector.scalar_tensor_tensor(out=x1l[:, cols], in0=l0[:, cols], scalar=b0c[:, 0:1],
                                               in1=x1h[:, cols].bitcast(F32), op0=ALU.add,
                                               op1=ALU.subtract).then_inc(x1l_made, 1)

            def sum_elements(n):
                to = sums0[:, bass.ds(n * GROUP_B, GROUP_B)]
                nc.vector.tensor_reduce(to, l0[:].rearrange("p (b d) -> p b d", d=D), AX.X,
                                        ALU.add).then_inc(l0_used, 1)

            def add_fields(tile, j, c):
                m = SUMMED.index(c)
                if m == 0:
                    dve.wait_ge(x2_made, x2_ready(tile - 2))
                dve.wait_ge(y_made, CHUNKS * tile + c + 1)
                for k in range(CF):
                    f = CF * c + k
                    to, of = acc[:, j % 2, k, :], y[c % YB][:, k * O:(k + 1) * O]
                    if m > 0 and k % 2 == 0:
                        dve.wait_ge(acc_step, SN * tile + (SN + CF * (m - 1) + k + 2))
                    if m == 0 and k > 0:
                        ins = nc.vector.tensor_scalar(to, of, x0t[:, j, f:f + 1], None, ALU.mult)
                    else:
                        ins = nc.vector.scalar_tensor_tensor(out=to, in0=of, scalar=x0t[:, j, f:f + 1],
                                                             in1=b1r[:] if m == 0 else to,
                                                             op0=ALU.mult, op1=ALU.add)
                    ins.then_inc(acc_step, 1)

            def body(n, kind):
                dve.wait_ge(x0t_made, 2 * n + 1)
                for e in range(TILES * CHUNKS):
                    j, c = divmod(e, CHUNKS)
                    if e == LOWER_AT and kind != "first":
                        lower(n, LAST)
                    if e == SUM_AT and kind != "first":
                        sum_elements(n)
                    if e == CHUNKS * (TILES - 1):
                        dve.wait_ge(x0t_made, 2 * n + 2)
                    if c in SUMMED:
                        add_fields(n * TILES + j, j, c)
                    if e == FIELDS_LOWER_AT[0]:
                        lower_fields(n, FIRST, kind == "first")
                    if e == FIELDS_LOWER_AT[1]:
                        lower_fields(n, LAST, kind == "first")
                    if c == X2L_AT and (kind != "first" or j > 0):
                        lower_x2(n * TILES + (j - 1), (j - 1) % 2)
                    if c == OWN_AT:
                        own_rows(n * TILES + j, j)
                    if e + LOWER_BEFORE in AHEAD_AT and kind != "last":
                        lower_product(n + 1, AHEAD_AT.index(e + LOWER_BEFORE))
                    if e == SPLIT_AT + LOWER_AFTER and kind != "last":
                        lower(n + 1, FIRST)

            dve.wait_ge(consts_made, 1)
            nc.vector.tensor_copy(own_r[:], own[:])
            nc.vector.tensor_tensor(own_half[:], own[:, 0:HALF_B], own[:, HALF_B:TILE_B], ALU.add).then_inc(own_made, 1)
            for k, (what, r, bank) in enumerate(PREP):
                if what == "l0":
                    lower_product(0, r)
                    continue
                dve.wait_ge(wh_made, turned_in(PREP[:k]) + 1)
                part, of = weights(w0l, w1l, what, r, bank)
                whole, _ = weights(w0h, w1h, what, r, bank)
                if (what, r) == ("w0", W0_STEPS - 1):
                    whole = part
                nc.vector.tensor_tensor(part, of, whole.bitcast(F32), ALU.subtract).then_inc(y_used[bank], 1)
            lower(0, FIRST)
            lower(0, LAST)
            sum_elements(0)
            groups(dve, body)
            lower_x2(GROUPS * TILES - 1, 1)
            dve.wait_ge(l0_used, GROUPS)
            nc.vector.tensor_scalar(sums0, sums0, b0d[:, 0:1], None, ALU.add).then_inc(sums_made, 1)
            for r in range(1, B // P, 2):
                dve.wait_ge(turned, r + 1)
                nc.vector.tensor_copy(outs[:, r, :], y[r][:, 0:L * O]).then_inc(outs_made[1], 1)

        @block.tensor
        def _(pe):
            pe.sem_inc(l2p_made, 2)

            def by_parts(to, xh, xl, wh, wl, first, last, x_stationary):
                for k, (a, b) in enumerate(((xh, wh), (xh, wl), (xl, wh))):
                    stationary, moving = (a, b) if x_stationary else (b, a)
                    ins = nc.tensor.matmul(to, stationary, moving, start=(first and k == 0), stop=(last and k == 2))
                return ins

            def layer0(n, t):
                rows, slot = z_rows(t), t % ZPARTS
                pe.wait_ge(zl_made, ZT * n + t + 1)
                if t == ZT - 1:
                    nc.tensor.matmul(l0[:], w0h[0:rows, t, :], zh[0:rows, slot, :], start=False,
                                     stop=True).then_inc(z_used, 1)
                    return
                by_parts(l0[:], zh[0:rows, slot, :], zl[0:rows, slot, :], w0h[0:rows, t, :], w0l[0:rows, t, :],
                         t == 0, False, False).then_inc(z_used, 1)

            def turn_fields():
                for j in range(TILES):
                    last = nc.tensor.transpose(xt[:, j, :], xg[0:F, j * P:(j + 1) * P], ident[0:F, 0:F])
                last.then_inc(xt_made, 1)

            def turn_w2(c):
                if c >= 2:
                    pe.wait_ge(w2_kept, c - 1)
                for k in range(CF):
                    last = nc.tensor.transpose(l2p[:, c % 2, k * O:(k + 1) * O],
                                               w2raw.rearrange("o (h f) -> o f h", f=F)[:, CF * c + k, :], ident[:])
                last.then_inc(w2_turned, 1)

            def quarter(q, part, fields_kept):
                if part == 0:
                    pe.wait_ge(l2p_used, q * (QG * TILES) + 1)
                    pe.wait_ge(x0t_made, fields_kept)
                each = F // QUARTER_PARTS
                for f in range(part * each, (part + 1) * each):
                    last = nc.tensor.matmul(l2, w2t[:, f, :], gram[:, f, :], start=(f == 0), stop=(f == F - 1))
                if part == QUARTER_PARTS - 1:
                    last.then_inc(l2_made, 1)

            def layer2(tile, slot):
                pe.wait_ge(x2l_made, tile + 1)
                pe.wait_ge(bdh_made, tile + 1)
                pe.wait_ge(bdl_made, tile + 1)
                pe.wait_ge(l2p_used, tile + 1)
                for k in range(2):
                    half = slice(k * HALF, (k + 1) * HALF)
                    by_parts(l2p[:, k, 0:HALF_B * F], x2h[half, slot], x2l[half, slot],
                             bdh[half, slot].rearrange("p b f -> p (b f)"),
                             bdl[half, slot].rearrange("p b f -> p (b f)"), True, True, True)
                nc.tensor.matmul(s1, x2h[:, slot], own_r[:], start=True, stop=False)
                nc.tensor.matmul(s1, x2l[:, slot], own_r[:], start=False, stop=True).then_inc(l2p_made, 1)

            def chunk(tile, j, c):
                before, late = (c - YB) % CHUNKS, c < YB
                if before in HELPED:
                    value = HN * tile + (HN + HELPED.index(before) + 1) - (HN if late else 0)
                    pe.wait_ge(prod_made, value)
                else:
                    value = SN * tile + (SN + CF * SUMMED.index(before) + CF) - (SN if late else 0)
                    pe.wait_ge(acc_step, value)
                cols = slice(j * P, (j + 1) * P)
                by_parts(y[c % YB][:], x1h[:, cols], x1l[:, cols], w1h[:, c, :], w1l[:, c, :],
                         True, True, True).then_inc(y_made, 1)

            pe.wait_ge(consts_made, 1)
            for k, (what, r, bank) in enumerate(PE_PREP):
                if what == "w0":
                    pe.wait_ge(pair_made, min(r, (POOL_PAIRS - 1) // 8) + 1)
                    if 8 * r + 8 > POOL_PAIRS:
                        pe.wait_ge(far_pair_made, 1)
                if what == "l0":
                    if r % 4 == 0:
                        pe.wait_ge(y_used[(r // 4) % YB], uses(PE_PREP[:r // 4 + 1], (r // 4) % YB))
                    layer0(0, r)
                    continue
                if (what, r) == ("w1", 0):
                    pe.wait_ge(w1_loaded, 16 * 8)
                if uses(PE_PREP[:k], bank):
                    pe.wait_ge(y_used[bank], uses(PE_PREP[:k], bank))
                if what == "w0":
                    for t in range(4 * r, min(4 * r + 4, ZT)):
                        rows = z_rows(t)
                        last = nc.tensor.transpose(y[bank][0:rows, (t % 4) * O:(t % 4 + 1) * O],
                                                   w0pair[:, t * P:t * P + rows], ident[:])
                else:
                    raw = w1raw.rearrange("o (h f) -> o f h", f=F)
                    for k4 in range(CF):
                        last = nc.tensor.transpose(y[bank][:, k4 * O:(k4 + 1) * O], raw[:, CF * r + k4, :], ident[:])
                last.then_inc(prep_made, 1)
            turn_fields()
            for i in range(YB):
                pe.wait_ge(y_used[i], uses(PE_PREP, i))

            def body(n, kind):
                for e in range(TILES * CHUNKS):
                    j, c = divmod(e, CHUNKS)
                    tile = n * TILES + j
                    if c == 0 and j in (0, TILES - 1):
                        pe.wait_ge(x1h_made, 2 * n + (2 if j else 1))
                        pe.wait_ge(x1l_made, 2 * n + (2 if j else 1))
                    if e == TURN_AT and kind != "last":
                        pe.wait_ge(x0t_made, 2 * n + 2)
                        pe.wait_ge(l2_used, (n // QG if kind == "inner" else 0) + 1)
                    chunk(tile, j, c)
                    if kind == "first" and W2_AT <= e < W2_AT + CHUNKS:
                        if e == W2_AT:
                            pe.wait_ge(w2_loaded, 16 * 8)
                        turn_w2(e - W2_AT)
                    if c == LAYER2_AT and (kind != "first" or j > 0):
                        if kind == "first" and j == 1:
                            pe.wait_ge(w2_kept, CHUNKS)
                        layer2(tile - 1, (j - 1) % 2)
                    if e in QUARTER_AT and kind == "inner":
                        with pe.If_eq(pe.to_reg(n % QG), 0):
                            quarter(n // QG, QUARTER_AT.index(e), 2 * n + 2)
                    if kind != "last":
                        if e == AHEAD_AT[0]:
                            pe.wait_ge(l0_used, n + 1)
                        if e in AHEAD_AT:
                            layer0(n + 1, AHEAD_AT.index(e))
                        if e == TURN_AT:
                            turn_fields()

            groups(pe, body)
            layer2(GROUPS * TILES - 1, 1)
            for part in range(QUARTER_PARTS):
                quarter(QUARTERS, part, 2 * GROUPS)

            pe.wait_ge(sums_made, 1)
            pe.wait_ge(l2_used, QUARTERS + 1)
            for r in range(B // P):
                for k in range(L):
                    last = nc.tensor.transpose(y[r][:, k * O:(k + 1) * O], sums[:, k, r * P:(r + 1) * P], ident[:])
                last.then_inc(turned, 1)


_INS = ["r_input", "L0_rec_W0", "L0_rec_b0", "L0_rec_W1", "L0_rec_b1", "L0_rec_W2", "L0_rec_b2"]
_OUTS = [((B, L * O), "float32")]


def kernel(**inputs):
    import numpy as _np
    import concourse.bacc as _bacc
    from concourse import mybir as _mybir
    from concourse.bass_utils import run_bass_kernel_spmd as _run

    nc = _bacc.Bacc("TRN2", target_bir_lowering=False, num_devices=1)
    arrays, args = {}, []
    for name in _INS:
        a = _np.ascontiguousarray(inputs[name])
        arrays[f"in_{name}_dram"] = a
        args.append(nc.dram_tensor(f"in_{name}_dram", a.shape, _mybir.dt.from_np(a.dtype), kind="ExternalInput").ap())
    for i, (shape, dtype) in enumerate(_OUTS):
        dt = _mybir.dt.from_np(_np.dtype(dtype))
        args.append(nc.dram_tensor(f"out_{i}_dram", shape, dt, kind="ExternalOutput").ap())
    cin_kernel(nc, *args)
    r = _run(nc, [arrays], core_ids=[0])
    got = tuple(r.results[0][f"out_{i}_dram"] for i in range(len(_OUTS)))
    return got[0]
```
